# Optimizing a Trainium2 kernel written in Bass

```python
import numpy as np
import jax
import jax.numpy as jnp

def _softmax(x, axis=-1):
    return jax.nn.softmax(x, axis=axis)
def _gelu(x):
    return jax.nn.gelu(x, approximate=True)
def _silu(x):
    return jax.nn.silu(x)
def _sigmoid(x):
    return jax.nn.sigmoid(x)
def _layernorm(x, axis=-1, eps=1e-5):
    m = jnp.mean(x, axis=axis, keepdims=True)
    v = jnp.var(x, axis=axis, keepdims=True)
    return (x - m) / jnp.sqrt(v + eps)
def _scatter_add(tgt, idx, src, axis=0):
    return tgt.at[idx].add(src)
def _segment_sum(src, seg, n):
    return jax.ops.segment_sum(src, seg, n)

kernel_name = 'mk_adj_preln_d1_adj_128_31e29c'

def setup_inputs(seed: int = 0):
    np.random.seed(seed)
    _w = jnp.asarray
    def _rec_inputs():
        import jax
        import jax.numpy as jnp
        _gk = jax.random.key(seed)
        x = -0.0002928 + 1 * jax.random.normal(jax.random.fold_in(_gk, 1), (8, 2048, 128), jnp.float32)
        _a = jax.random.bernoulli(jax.random.fold_in(_gk, 2), 0.00195312, (2048, 2048))
        _a = jnp.logical_or(_a, jnp.swapaxes(_a, -1, -2))
        _a = jnp.logical_or(_a, jnp.eye(2048, dtype=bool))
        _af = _a.astype(jnp.float32)
        _af = _af * jax.random.uniform(jax.random.fold_in(_gk, 3), (2048, 2048), jnp.float32, 0.05, 0.0846872)
        adj = _af
        return x, adj
    x, adj = _rec_inputs()
    def _L0_gnn_setup():
        import jax, jax.numpy as jnp
        import numpy as np
        from jax import lax
        CONV_ORDER = 3

        def _chebyshev(adj, x, order):

            def step(carry, _):
                nxt = jnp.einsum('ij,bjc->bic', adj, carry)
                return (nxt, nxt)
            _, xs = lax.scan(step, x, None, length=order)
            return jnp.moveaxis(xs, 0, -1)
        key = jax.random.key(seed)
        k1, k2, k3, k4 = jax.random.split(key, 4)
        B, E, C_in, C_out, K, n_adjs = (8, 4096, 128, 128, CONV_ORDER, 2)
        x_1 = jax.random.normal(k1, (B, E, C_in), dtype=jnp.float32)
        adj0 = jax.random.normal(k2, (E, E), dtype=jnp.float32) / np.sqrt(E)
        adj1 = jax.random.normal(k3, (E, E), dtype=jnp.float32) / np.sqrt(E)
        kdim = K * n_adjs + 1
        std = 1.414 * np.sqrt(2.0 / float((C_in + C_out) * kdim))
        weight_1 = std * jax.random.normal(k4, (C_in, C_out, kdim), dtype=jnp.float32)
        return {'x_1': x_1, 'adj0': adj0, 'adj1': adj1, 'weight_1': weight_1}
    _L0_gnn_all = _L0_gnn_setup()
    _L0_gnn_in = {k: v for k, v in _L0_gnn_all.items() if k in ('weight_1', )}
    del _L0_gnn_all

    return {
        "x": x,
        "adj": adj,
        "L0_gnn_weight_1": _L0_gnn_in["weight_1"],
    }

def reference(x, adj, L0_gnn_weight_1):
    import jax
    import jax.numpy as jnp
    def _L0_gnn_ref(x_1, adj0, adj1, weight_1):
        import jax, jax.numpy as jnp
        import numpy as np
        from jax import lax
        CONV_ORDER = 3

        def _chebyshev(adj, x, order):

            def step(carry, _):
                nxt = jnp.einsum('ij,bjc->bic', adj, carry)
                return (nxt, nxt)
            _, xs = lax.scan(step, x, None, length=order)
            return jnp.moveaxis(xs, 0, -1)
        parts = [x_1[..., None], _chebyshev(adj0, x_1, CONV_ORDER), _chebyshev(adj1, x_1, CONV_ORDER)]
        x_all = jnp.concatenate(parts, axis=3)
        y_1 = jnp.einsum('bnik,iok->bno', x_all, weight_1)
        return y_1

    h = jnp.maximum(_layernorm(x, axis=-1), 0.0)
    x = x + _L0_gnn_ref(h, adj, adj, L0_gnn_weight_1)
    return x


_drawn_inputs = setup_inputs


def setup_inputs(seed=0):
    import zlib

    import numpy as np

    out = dict(_drawn_inputs(seed))
    spreads = {}
    factors = {}
    for name, (base, spread) in spreads.items():
        noise = np.random.default_rng([zlib.crc32(name.encode()), seed]).standard_normal(out[name].shape)
        drawn = base * np.exp(spread * noise) if base else spread * noise
        out[name] = jnp.asarray(drawn.astype(out[name].dtype))
    for name, factor in factors.items():
        out[name] = (out[name] * factor).astype(out[name].dtype)
    return out
```

```python
from contextlib import ExitStack

import concourse.bass as bass
import concourse.mybir as mybir

P = 128
B, N, C = 8, 2048, 128
NB = N // P
HB = B // 2
W = HB * C
PW = W // 2
TERMS = 4
HOPS = 3
STAGES = 2 * HOPS
PAIRS = NB // 2
CH = NB * P // 2
EPS = 1e-5

F32 = mybir.dt.float32
F32R = mybir.dt.float32r
ALU = mybir.AluOpType
ACT = mybir.ActivationFunctionType


def build(nc, x, adj, weight, out):
    ctx = ExitStack()
    with ctx:
        def sb(name, shape, dt=F32):
            return ctx.enter_context(nc.sbuf_tensor(name, shape, dt))

        def pb(name, shape):
            return ctx.enter_context(nc.psum_tensor(name, shape, F32))

        def sem(name):
            return ctx.enter_context(nc.semaphore(name))

        def sems(name):
            return [sem(f"{name}{slot}") for slot in range(2)]

        spill = nc.dram_tensor("y_spill", [2 * NB, P, 3 * W], F32, kind="Internal").ap()

        u_hi = sb("u_hi", [P, 2, NB, W], F32R)
        u_lo = sb("u_lo", [P, 2, NB, W], F32R)
        a_raw = sb("a_raw", [P, 2, CH])
        a_hi = sb("a_hi", [P, 2, NB * P], F32R)
        a_lo = sb("a_lo", [P, 2, NB * P], F32R)
        y_in = sb("y_in", [P, 2, W])
        x_res = sb("x_res", [P, 2, W])
        u_sum = sb("u_sum", [P, W])
        x_in = sb("x_in", [P, 2, W])
        x_norm = sb("x_norm", [P, 2, PW])
        ht_hi = sb("ht_hi", [P, 2, PW], F32R)
        ht_lo = sb("ht_lo", [P, 2, PW], F32R)
        y_out = sb("y_out", [P, 2, 3 * W])
        v_hi = sb("v_hi", [P, TERMS * C], F32R)
        v_lo = sb("v_lo", [P, TERMS * C], F32R)
        ident = sb("ident", [P, P])
        bn = sb("bn", [P, 2, 6])
        mean_var = sb("mean_var", [P, 2, 2, 2])
        std = sb("std", [P, 2, 2])
        rstd = sb("rstd", [P, 2])
        eps = sb("eps", [P, 1])
        w_raw = y_out[:, 0, :]

        ps_hop = [pb(f"ps_hop{s}", [P, W]) for s in range(2)]
        ps_turn = [pb(f"ps_turn{s}", [P, 512]) for s in range(2)]
        ps_proj = [pb(f"ps_proj{s}", [P, 2, TERMS * C]) for s in range(2)]

        w_landed = sem("w_landed")
        w_summed = sem("w_summed")
        v_hi_ready = sem("v_hi_ready")
        v_ready = sem("v_ready")
        ident_zero = sem("ident_zero")
        ident_ready = sem("ident_ready")
        eps_ready = sem("eps_ready")
        x_landed = sems("x_landed")
        x_used = sems("x_used")
        bn_ready = sem("bn_ready")
        stats_ready = sems("stats_ready")
        std_ready = sems("std_ready")
        rstd_ready = sem("rstd_ready")
        norm_ready = sems("norm_ready")
        turned = sems("turned")
        ht_hi_ready = sems("ht_hi_ready")
        ht_ready = sems("ht_ready")
        projected = sems("projected")
        proj_hi_ready = sems("proj_hi_ready")
        proj_ready = sems("proj_ready")
        spilled = sems("spilled")
        a_landed = sems("a_landed")
        a_hi_ready = sems("a_hi_ready")
        a_ready = sems("a_ready")
        hop_done = sems("hop_done")
        y_landed = sems("y_landed")
        res_landed = sems("res_landed")
        summed = sems("summed")
        u_hi_ready = sem("u_hi_ready")
        u_ready = sem("u_ready")
        out_ready = sems("out_ready")
        stored = sem("stored")

        def final(s):
            return s % HOPS == HOPS - 1

        def inner_before(s):
            return NB * (s - s // HOPS)

        def ds(start, size):
            return bass.ds(start, size)

        def rows(tensor, copy, ib):
            return tensor[:, copy, ds(ib, 1), :].rearrange("p a w -> p (a w)")

        def pair_rows(tensor, copy, ib, w):
            return tensor[:, copy, ds(ib, 1), w * PW:(w + 1) * PW].rearrange("p a (b c) -> p (a b) c", b=2)

        def pair_terms(v, w):
            return y_out[:, v, :].rearrange("p (k q b c) -> p k q b c", k=3, q=2, b=2)[:, :, w]

        block = ctx.enter_context(nc.Block())

        @block.sync
        def _(sp):
            def load_x(unit, v, turn):
                if not (isinstance(turn, int) and turn == 0):
                    sp.wait_ge(x_used[v], 2 * turn)
                sp.dma_start(x_in[:, v, :], x[ds(unit, 1), :, :].rearrange("a p w -> (a p) w")
                             ).then_inc(x_landed[v], 16)

            def load_a(ib, u, turn):
                for c in range(2):
                    if turn is not None:
                        sp.wait_ge(a_ready[u], 2 * turn + c + 1)
                    sp.dma_start(a_raw[:, c, :],
                                 adj[ds(ib, 1), :, c * CH:(c + 1) * CH].rearrange("a p w -> (a p) w")
                                 ).then_inc(a_landed[c], 16)

            def load_y(s, ib, u):
                k = HOPS - 1 - s % HOPS
                unit = NB * (s // HOPS) + ib
                sp.dma_start(y_in[:, u, :],
                             spill[ds(unit, 1), :, k * W:(k + 1) * W].rearrange("a p w -> (a p) w")
                             ).then_inc(y_landed[u], 16)
                if final(s):
                    sp.dma_start(x_res[:, u, :], x[ds(unit, 1), :, :].rearrange("a p w -> (a p) w")
                                 ).then_inc(res_landed[u], 16)

            sp.dma_start(w_raw[:, 0:7 * C], weight).then_inc(w_landed, 16)
            load_x(0, 0, 0)
            load_x(1, 1, 0)
            load_a(0, 0, None)
            with sp.Fori(0, PAIRS) as i:
                for v in range(2):
                    load_x(2 * i + 2 + v, v, i + 1)

            for s in range(STAGES):
                n0 = PAIRS * s
                proj = s == HOPS - 1
                if s % HOPS == 0:
                    for v in range(2):
                        sp.wait_ge(spilled[v], 16 * PAIRS * (s // HOPS + 1))
                if s == 0:
                    load_y(s, 0, 0)
                if final(s):
                    sp.wait_ge(summed[1], n0)

                def turn(i, last):
                    n = n0 + i
                    for u in range(2):
                        if u == 0:
                            nxt = (s, 2 * i + 1)
                        elif not last:
                            nxt = (s, 2 * i + 2)
                        elif s < STAGES - 1:
                            nxt = (s + 1, 0)
                        else:
                            break
                        load_a(nxt[1], u, n)
                        if nxt[0] % HOPS == 0 and nxt[0] != s:
                            for v in range(2):
                                sp.wait_ge(spilled[v], 16 * PAIRS * (nxt[0] // HOPS + 1))
                        if final(s) and s == nxt[0]:
                            sp.wait_ge(out_ready[1 - u], PAIRS * (s // HOPS) + i + u)
                        elif not (u == 0 and isinstance(n, int) and n == 0):
                            sp.wait_ge(summed[1 - u], n + u)
                        load_y(*nxt, 1 - u)
                        if proj and not last:
                            load_x(NB + 2 * i + 2 + u, u, PAIRS + i + 1)

                with sp.Fori(0, PAIRS - 1) as i:
                    turn(i, False)
                turn(PAIRS - 1, True)

        @block.gpsimd
        def _(pool):
            nc.gpsimd.memset(ident[:], 0.0).then_inc(ident_zero, 1)
            nc.gpsimd.memset(eps[:], EPS).then_inc(eps_ready, 1)
            pool.wait_ge(ident_zero, 1)
            nc.gpsimd.affine_select(out=ident[:], in_=ident[:], compare_op=ALU.not_equal, fill=1.0,
                                    base=0, pattern=[[-1, P]], channel_multiplier=1
                                    ).then_inc(ident_ready, 1)

            def store_y(unit, v):
                for w in range(2):
                    pool.wait_ge(proj_hi_ready[w], unit + 1)
                pool.dma_start(spill[ds(unit, 1), :, :].rearrange("a p w -> (a p) w"),
                               y_out[:, v, :]).then_inc(spilled[v], 16)

            def store_out(unit, u, m):
                pool.wait_ge(out_ready[u], m + 1)
                pool.dma_start(out[ds(unit, 1), :, :].rearrange("a p w -> (a p) w"),
                               u_sum[:]).then_inc(stored, 16)

            with pool.Fori(0, PAIRS) as i:
                for v in range(2):
                    store_y(2 * i + v, v)
            with pool.Fori(0, PAIRS) as i:
                for v in range(2):
                    store_out(2 * i + v, v, i)
                    store_y(NB + 2 * i + v, v)
            with pool.Fori(0, PAIRS) as i:
                for v in range(2):
                    store_out(NB + 2 * i + v, v, PAIRS + i)
            pool.wait_ge(stored, 16 * 2 * NB)

        @block.tensor
        def _(pe):
            def turn_pair(w, unit):
                pe.wait_ge(norm_ready[w], unit + 1)
                pe.wait_ge(ht_ready[w], unit)
                for b in range(2):
                    last = nc.tensor.transpose(ps_turn[w][:, b * P:(b + 1) * P],
                                               x_norm[:, w, b * C:(b + 1) * C], ident[:])
                last.then_inc(turned[w], 1)

            def project(w, unit):
                pe.wait_ge(ht_ready[w], unit + 1)
                pe.wait_ge(proj_ready[w], unit)
                for b in range(2):
                    cols = slice(b * P, (b + 1) * P)
                    for n, (h, v) in enumerate(((ht_hi, v_lo), (ht_hi, v_hi), (ht_lo, v_hi))):
                        last = nc.tensor.matmul(ps_proj[w][:, b, :], h[:, w, cols], v[:],
                                                start=n == 0, stop=n == 2)
                last.then_inc(projected[w], 1)

            def hop(s, u, n):
                r = s % 2
                pe.wait_ge(summed[u], n)
                for jb in range(NB):
                    if jb in (0, NB // 2):
                        pe.wait_ge(a_ready[u], 2 * n + 1 + jb // (NB // 2))
                    if jb in (0, NB - 2, NB - 1):
                        rows = NB - 2 if jb == 0 else jb + 1
                        if s % HOPS:
                            pe.wait_ge(u_ready, inner_before(s) - NB + rows)
                        elif jb == 0:
                            for w in range(2):
                                pe.wait_ge(proj_ready[w], NB * (s // HOPS + 1))
                    cols = slice(jb * P, (jb + 1) * P)
                    nc.tensor.matmul(ps_hop[u][:], a_hi[:, u, cols], u_lo[:, r, jb, :],
                                     start=jb == 0, stop=False)
                    nc.tensor.matmul(ps_hop[u][:], a_hi[:, u, cols], u_hi[:, r, jb, :],
                                     start=False, stop=False)
                    last = nc.tensor.matmul(ps_hop[u][:], a_lo[:, u, cols], u_hi[:, r, jb, :],
                                            start=False, stop=jb == NB - 1)
                last.then_inc(hop_done[u], 1)

            pe.wait_ge(ident_ready, 1)
            turn_pair(0, 0)
            pe.wait_ge(v_ready, 1)
            with pe.Fori(0, NB) as unit:
                turn_pair(1, unit)
                project(0, unit)
                turn_pair(0, unit + 1)
                project(1, unit)
            for s in range(STAGES):
                if s != HOPS - 1:
                    with pe.Fori(0, PAIRS) as i:
                        for u in range(2):
                            hop(s, u, PAIRS * s + i)
                    continue

                def turn(i, last):
                    for u in range(2):
                        unit = NB + 2 * i + u
                        turn_pair(1, unit)
                        hop(s, u, PAIRS * s + i)
                        project(0, unit)
                        if not (last and u == 1):
                            turn_pair(0, unit + 1)
                        project(1, unit)

                with pe.Fori(0, PAIRS - 1) as i:
                    turn(i, False)
                turn(PAIRS - 1, True)

        @block.scalar
        def _(act):
            def relu_turned(w, unit):
                act.wait_ge(turned[w], unit + 1)
                act.wait_ge(projected[w], unit)
                nc.scalar.activation(ht_hi[:, w, :], ps_turn[w][:, 0:PW], ACT.Relu
                                     ).then_inc(ht_hi_ready[w], 1)

            def std_dev(w, unit):
                act.wait_ge(stats_ready[w], unit + 1)
                nc.scalar.activation(std[:, w, :], mean_var[:, w, :, 1], ACT.Sqrt, bias=eps[:]
                                     ).then_inc(std_ready[w], 1)

            def proj_hi(write, ib, w, unit, v, turn):
                act.wait_ge(projected[w], unit + 1)
                nc.scalar.activation(pair_rows(u_hi, write, ib, w), ps_proj[w][:, :, 3 * C:4 * C], ACT.Copy)
                act.wait_ge(spilled[v], 16 * turn)
                nc.scalar.activation(pair_terms(v, w), ps_proj[w][:, :, 0:3 * C].rearrange(
                    "p b (k c) -> p k b c", k=3), ACT.Copy).then_inc(proj_hi_ready[w], 1)

            def split_hi(u, n):
                act.wait_ge(hop_done[u], n)
                for c in range(2):
                    blocks = 2 * n + u + 1
                    act.wait_ge(a_landed[c], 16 * blocks)
                    nc.scalar.activation(a_hi[:, u, c * CH:(c + 1) * CH], a_raw[:, c, :], ACT.Copy
                                         ).then_inc(a_hi_ready[u], 1)

            def hop_hi(s, u, n, ib):
                act.wait_ge(summed[u], n + 1)
                nc.scalar.activation(rows(u_hi, (s + 1) % 2, ib), u_sum[:], ACT.Copy
                                     ).then_inc(u_hi_ready, 1)

            act.wait_ge(eps_ready, 1)
            std_dev(0, 0)
            act.wait_ge(w_summed, 1)
            nc.scalar.activation(v_hi[:], w_raw[:, 0:TERMS * C], ACT.Copy).then_inc(v_hi_ready, 1)
            std_dev(1, 0)
            relu_turned(0, 0)

            def project_turn(i):
                for v in range(2):
                    unit = 2 * i + v
                    relu_turned(1, unit)
                    std_dev(0, unit + 1)
                    proj_hi(0, unit, 0, unit, v, i)
                    relu_turned(0, unit + 1)
                    std_dev(1, unit + 1)
                    proj_hi(0, unit, 1, unit, v, i)

            with act.Fori(0, PAIRS // 2) as i:
                project_turn(i)
            split_hi(0, 0)
            with act.Fori(PAIRS // 2, PAIRS) as i:
                project_turn(i)

            for s in range(STAGES):
                proj = s == HOPS - 1

                def turn(i, last):
                    n = PAIRS * s + i
                    for u in range(2):
                        ib = 2 * i + u
                        unit = NB + ib
                        end = last and u == 1
                        if proj:
                            relu_turned(1, unit)
                            if not end:
                                std_dev(0, unit + 1)
                        if not (s == STAGES - 1 and end):
                            split_hi(1 - u, n + u)
                        if not final(s):
                            hop_hi(s, u, n, ib)
                        if proj:
                            proj_hi((s + 1) % 2, ib, 0, unit, u, PAIRS + i)
                            if not end:
                                relu_turned(0, unit + 1)
                                std_dev(1, unit + 1)
                            proj_hi((s + 1) % 2, ib, 1, unit, u, PAIRS + i)

                if final(s):
                    with act.Fori(0, PAIRS - 1) as i:
                        turn(i, False)
                    turn(PAIRS - 1, True)
                else:
                    with act.Fori(0, PAIRS) as i:
                        turn(i, False)

        @block.vector
        def _(dve):
            def stats(w, unit, v, turn, between=None):
                dve.wait_ge(x_landed[v], 16 * (turn + 1))
                dve.wait_ge(stats_ready[1 - w], unit + w)
                dve.wait_ge(norm_ready[w], unit)
                for b in range(2):
                    last = nc.vector.bn_stats(bn[:, b, :], x_in[:, v, w * PW + b * C:w * PW + (b + 1) * C])
                last.then_inc(bn_ready, 1)
                dve.wait_ge(bn_ready, 2 * unit + w + 1)
                if between:
                    turned_lo(*between)
                for b in range(2):
                    last = nc.vector.bn_aggr(mean_var[:, w, b, :], bn[:, b, :])
                last.then_inc(stats_ready[w], 1)

            def normalise(w, unit, v):
                dve.wait_ge(std_ready[w], unit + 1)
                dve.wait_ge(norm_ready[1 - w], unit + w)
                nc.vector.reciprocal(rstd[:], std[:, w, :]).then_inc(rstd_ready, 1)
                dve.wait_ge(turned[w], unit)
                dve.wait_ge(rstd_ready, 2 * unit + w + 1)
                for b in range(2):
                    last = nc.vector.tensor_scalar(x_norm[:, w, b * C:(b + 1) * C],
                                                   x_in[:, v, w * PW + b * C:w * PW + (b + 1) * C],
                                                   mean_var[:, w, b, 0:1], rstd[:, b:b + 1],
                                                   ALU.subtract, ALU.mult)
                last.then_inc(norm_ready[w], 1)
                dve.wait_ge(norm_ready[w], unit + 1)
                dve.sem_inc(x_used[v], 1)

            def turned_lo(w, unit):
                dve.wait_ge(ht_hi_ready[w], unit + 1)
                nc.vector.scalar_tensor_tensor(out=ht_lo[:, w, :], in0=ps_turn[w][:, 0:PW], scalar=0.0,
                                               in1=ht_hi[:, w, :].bitcast(F32), op0=ALU.max,
                                               op1=ALU.subtract).then_inc(ht_ready[w], 1)

            def proj_lo(write, ib, w, unit):
                dve.wait_ge(proj_hi_ready[w], unit + 1)
                nc.vector.tensor_tensor(pair_rows(u_lo, write, ib, w), ps_proj[w][:, :, 3 * C:4 * C],
                                        pair_rows(u_hi, write, ib, w).bitcast(F32), ALU.subtract
                                        ).then_inc(proj_ready[w], 1)

            def split_lo(u, n):
                for c in range(2):
                    cols = slice(c * CH, (c + 1) * CH)
                    dve.wait_ge(a_hi_ready[u], 2 * n + c + 1)
                    nc.vector.tensor_tensor(a_lo[:, u, cols], a_raw[:, c, :],
                                            a_hi[:, u, cols].bitcast(F32), ALU.subtract
                                            ).then_inc(a_ready[u], 1)

            def hop_sum(s, u, n, ib):
                dve.wait_ge(hop_done[u], n + 1)
                dve.wait_ge(y_landed[u], 16 * (n + 1))
                if final(s):
                    dve.wait_ge(stored, 16 * (NB * (s // HOPS) + ib))
                else:
                    dve.wait_ge(u_ready, inner_before(s) + ib)
                nc.vector.tensor_tensor(u_sum[:], ps_hop[u][:], y_in[:, u, :], ALU.add
                                        ).then_inc(summed[u], 1)
                if final(s):
                    m = n - PAIRS * s + PAIRS * (s // HOPS)
                    dve.wait_ge(res_landed[u], 16 * (m + 1))
                    dve.wait_ge(summed[u], n + 1)
                    nc.vector.tensor_tensor(u_sum[:], u_sum[:], x_res[:, u, :], ALU.add
                                            ).then_inc(out_ready[u], 1)
                else:
                    dve.wait_ge(u_hi_ready, inner_before(s) + ib + 1)
                    nc.vector.tensor_tensor(rows(u_lo, (s + 1) % 2, ib), u_sum[:],
                                            rows(u_hi, (s + 1) % 2, ib).bitcast(F32), ALU.subtract
                                            ).then_inc(u_ready, 1)

            stats(0, 0, 0, 0)
            dve.wait_ge(w_landed, 16)
            nc.vector.tensor_tensor(w_raw[:, C:4 * C], w_raw[:, C:4 * C], w_raw[:, 4 * C:7 * C], ALU.add
                                    ).then_inc(w_summed, 1)
            normalise(0, 0, 0)
            dve.wait_ge(v_hi_ready, 1)
            nc.vector.tensor_tensor(v_lo[:], w_raw[:, 0:4 * C], v_hi[:].bitcast(F32), ALU.subtract
                                    ).then_inc(v_ready, 1)
            stats(1, 0, 0, 0)
            normalise(1, 0, 0)
            turned_lo(0, 0)

            def project_turn(i):
                for v in range(2):
                    unit = 2 * i + v
                    stats(0, unit + 1, 1 - v, i + v, between=(1, unit))
                    normalise(0, unit + 1, 1 - v)
                    proj_lo(0, unit, 0, unit)
                    stats(1, unit + 1, 1 - v, i + v, between=(0, unit + 1))
                    normalise(1, unit + 1, 1 - v)
                    proj_lo(0, unit, 1, unit)

            with dve.Fori(0, PAIRS // 2) as i:
                project_turn(i)
            split_lo(0, 0)
            with dve.Fori(PAIRS // 2, PAIRS) as i:
                project_turn(i)

            for s in range(STAGES):
                proj = s == HOPS - 1
                if final(s):
                    dve.wait_ge(u_ready, inner_before(s))
                if s == HOPS:
                    dve.wait_ge(stored, 16 * NB)

                def turn(i, last):
                    n = PAIRS * s + i
                    for u in range(2):
                        ib = 2 * i + u
                        unit = NB + ib
                        end = last and u == 1
                        if proj:
                            if end:
                                turned_lo(1, unit)
                            else:
                                stats(0, unit + 1, 1 - u, PAIRS + i + u, between=(1, unit))
                                normalise(0, unit + 1, 1 - u)
                        if not (s == STAGES - 1 and end):
                            split_lo(1 - u, n + u)
                        hop_sum(s, u, n, ib)
                        if proj:
                            proj_lo((s + 1) % 2, ib, 0, unit)
                            if not end:
                                stats(1, unit + 1, 1 - u, PAIRS + i + u, between=(0, unit + 1))
                                normalise(1, unit + 1, 1 - u)
                            proj_lo((s + 1) % 2, ib, 1, unit)

                if final(s):
                    with dve.Fori(0, PAIRS - 1) as i:
                        turn(i, False)
                    turn(PAIRS - 1, True)
                else:
                    with dve.Fori(0, PAIRS) as i:
                        turn(i, False)


def kernel(x, adj, L0_gnn_weight_1):
    import numpy as np
    import concourse.bacc as bacc
    from concourse.bass_utils import run_bass_kernel_spmd

    x_units = np.ascontiguousarray(
        x.reshape(2, HB, NB, P, C).transpose(0, 2, 3, 1, 4)).reshape(2 * NB, P, W)
    panels = np.ascontiguousarray(
        adj.reshape(NB, P, NB, P).transpose(0, 3, 2, 1)).reshape(NB, P, NB * P)
    weight = np.ascontiguousarray(L0_gnn_weight_1.transpose(0, 2, 1)).reshape(C, 7 * C)

    nc = bacc.Bacc("TRN2", target_bir_lowering=False, num_devices=1)
    arrays = {"x_units": x_units, "panels": panels, "weight": weight}
    args = [nc.dram_tensor(name, a.shape, F32, kind="ExternalInput").ap() for name, a in arrays.items()]
    out = nc.dram_tensor("out", (2 * NB, P, W), F32, kind="ExternalOutput").ap()
    build(nc, *args, out)
    got = run_bass_kernel_spmd(nc, [arrays], core_ids=[0]).results[0]["out"]
    return got.reshape(2, NB, P, HB, C).transpose(0, 3, 1, 2, 4).reshape(B, N, C)
```

```python
from contextlib import ExitStack

import concourse.bass as bass
import concourse.mybir as mybir

P = 128
B, N, C = 8, 2048, 128
NB = N // P
HB = B // 2
W = HB * C
PW = W // 2
TERMS = 4
HOPS = 3
STAGES = 2 * HOPS
PAIRS = NB // 2
CH = NB * P // 2
EPS = 1e-5

F32 = mybir.dt.float32
F32R = mybir.dt.float32r
ALU = mybir.AluOpType
ACT = mybir.ActivationFunctionType


def build(nc, x, adj, weight, out):
    ctx = ExitStack()
    with ctx:
        def sb(name, shape, dt=F32):
            return ctx.enter_context(nc.sbuf_tensor(name, shape, dt))

        def pb(name, shape):
            return ctx.enter_context(nc.psum_tensor(name, shape, F32))

        def sem(name):
            return ctx.enter_context(nc.semaphore(name))

        def sems(name):
            return [sem(f"{name}{slot}") for slot in range(2)]

        spill = nc.dram_tensor("y_spill", [2 * NB, P, 3 * W], F32, kind="Internal").ap()

        u_hi = sb("u_hi", [P, 2, NB, W], F32R)
        u_lo = sb("u_lo", [P, 2, NB, W], F32R)
        a_raw = sb("a_raw", [P, 2, CH])
        a_hi = sb("a_hi", [P, 2, NB * P], F32R)
        a_lo = sb("a_lo", [P, 2, NB * P], F32R)
        y_in = sb("y_in", [P, 2, W])
        x_res = sb("x_res", [P, 2, W])
        u_sum = sb("u_sum", [P, W])
        x_in = sb("x_in", [P, 2, W])
        x_norm = sb("x_norm", [P, 2, W])
        ht_hi = sb("ht_hi", [P, 2, PW], F32R)
        ht_lo = sb("ht_lo", [P, 2, PW], F32R)
        y_out = sb("y_out", [P, 2, 3 * W])
        v_hi = sb("v_hi", [P, TERMS * C], F32R)
        v_lo = sb("v_lo", [P, TERMS * C], F32R)
        ident = sb("ident", [P, P])
        bn = sb("bn", [P, HB, 6])
        mean_var = sb("mean_var", [P, HB, 2])
        std = sb("std", [P, HB])
        rstd = sb("rstd", [P, HB])
        eps = sb("eps", [P, 1])
        w_raw = y_out[:, 0, :]

        ps_hop = [pb(f"ps_hop{s}", [P, W]) for s in range(2)]
        ps_turn = [pb(f"ps_turn{s}", [P, 512]) for s in range(2)]
        ps_proj = [pb(f"ps_proj{s}", [P, 2, TERMS * C]) for s in range(2)]

        w_landed = sem("w_landed")
        w_summed = sem("w_summed")
        v_hi_ready = sem("v_hi_ready")
        v_ready = sem("v_ready")
        ident_zero = sem("ident_zero")
        ident_ready = sem("ident_ready")
        eps_ready = sem("eps_ready")
        x_landed = sems("x_landed")
        bn_ready = sem("bn_ready")
        stats_ready = sem("stats_ready")
        std_ready = sem("std_ready")
        rstd_ready = sem("rstd_ready")
        norm_ready = sems("norm_ready")
        turned = sems("turned")
        ht_hi_ready = sems("ht_hi_ready")
        ht_ready = sems("ht_ready")
        projected = sems("projected")
        proj_hi_ready = sems("proj_hi_ready")
        proj_ready = sems("proj_ready")
        spilled = sems("spilled")
        a_landed = sems("a_landed")
        a_hi_ready = sems("a_hi_ready")
        a_ready = sems("a_ready")
        hop_done = sems("hop_done")
        y_landed = sems("y_landed")
        res_landed = sems("res_landed")
        summed = sems("summed")
        u_hi_ready = sem("u_hi_ready")
        u_ready = sem("u_ready")
        out_ready = sems("out_ready")
        stored = sem("stored")

        def final(s):
            return s % HOPS == HOPS - 1

        def inner_before(s):
            return NB * (s - s // HOPS)

        def ds(start, size):
            return bass.ds(start, size)

        def rows(tensor, copy, ib):
            return tensor[:, copy, ds(ib, 1), :].rearrange("p a w -> p (a w)")

        def pair_rows(tensor, copy, ib, w):
            return tensor[:, copy, ds(ib, 1), w * PW:(w + 1) * PW].rearrange("p a (b c) -> p (a b) c", b=2)

        def pair_terms(v, w):
            return y_out[:, v, :].rearrange("p (k q b c) -> p k q b c", k=3, q=2, b=2)[:, :, w]

        block = ctx.enter_context(nc.Block())

        @block.sync
        def _(sp):
            def load_x(unit, v, turn):
                if turn is not None:
                    sp.wait_ge(norm_ready[v], turn)
                sp.dma_start(x_in[:, v, :], x[ds(unit, 1), :, :].rearrange("a p w -> (a p) w")
                             ).then_inc(x_landed[v], 16)

            def load_a(ib, u, turn):
                for c in range(2):
                    if turn is not None:
                        sp.wait_ge(a_ready[u], 2 * turn + c + 1)
                    sp.dma_start(a_raw[:, c, :],
                                 adj[ds(ib, 1), :, c * CH:(c + 1) * CH].rearrange("a p w -> (a p) w")
                                 ).then_inc(a_landed[c], 16)

            def load_y(s, ib, u):
                k = HOPS - 1 - s % HOPS
                unit = NB * (s // HOPS) + ib
                sp.dma_start(y_in[:, u, :],
                             spill[ds(unit, 1), :, k * W:(k + 1) * W].rearrange("a p w -> (a p) w")
                             ).then_inc(y_landed[u], 16)
                if final(s):
                    sp.dma_start(x_res[:, u, :], x[ds(unit, 1), :, :].rearrange("a p w -> (a p) w")
                                 ).then_inc(res_landed[u], 16)

            sp.dma_start(w_raw[:, 0:7 * C], weight).then_inc(w_landed, 16)
            load_x(0, 0, None)
            load_x(1, 1, None)
            load_a(0, 0, None)
            with sp.Fori(0, PAIRS) as i:
                for v in range(2):
                    load_x(2 * i + 2 + v, v, i + 1)

            for s in range(STAGES):
                n0 = PAIRS * s
                proj = s == HOPS - 1
                if s % HOPS == 0:
                    for v in range(2):
                        sp.wait_ge(spilled[v], 16 * PAIRS * (s // HOPS + 1))
                if s == 0:
                    load_y(s, 0, 0)
                if final(s):
                    sp.wait_ge(summed[1], n0)

                def turn(i, last):
                    n = n0 + i
                    for u in range(2):
                        if u == 0:
                            nxt = (s, 2 * i + 1)
                        elif not last:
                            nxt = (s, 2 * i + 2)
                        elif s < STAGES - 1:
                            nxt = (s + 1, 0)
                        else:
                            break
                        load_a(nxt[1], u, n)
                        if nxt[0] % HOPS == 0 and nxt[0] != s:
                            for v in range(2):
                                sp.wait_ge(spilled[v], 16 * PAIRS * (nxt[0] // HOPS + 1))
                        if final(s) and s == nxt[0]:
                            sp.wait_ge(out_ready[1 - u], PAIRS * (s // HOPS) + i + u)
                        elif not (u == 0 and isinstance(n, int) and n == 0):
                            sp.wait_ge(summed[1 - u], n + u)
                        load_y(*nxt, 1 - u)
                        if proj and not last:
                            load_x(NB + 2 * i + 2 + u, u, PAIRS + i + 1)

                with sp.Fori(0, PAIRS - 1) as i:
                    turn(i, False)
                turn(PAIRS - 1, True)

        @block.gpsimd
        def _(pool):
            nc.gpsimd.memset(ident[:], 0.0).then_inc(ident_zero, 1)
            nc.gpsimd.memset(eps[:], EPS).then_inc(eps_ready, 1)
            pool.wait_ge(ident_zero, 1)
            nc.gpsimd.affine_select(out=ident[:], in_=ident[:], compare_op=ALU.not_equal, fill=1.0,
                                    base=0, pattern=[[-1, P]], channel_multiplier=1
                                    ).then_inc(ident_ready, 1)

            def store_y(unit, v):
                for w in range(2):
                    pool.wait_ge(proj_hi_ready[w], unit + 1)
                pool.dma_start(spill[ds(unit, 1), :, :].rearrange("a p w -> (a p) w"),
                               y_out[:, v, :]).then_inc(spilled[v], 16)

            def store_out(unit, u, m):
                pool.wait_ge(out_ready[u], m + 1)
                pool.dma_start(out[ds(unit, 1), :, :].rearrange("a p w -> (a p) w"),
                               u_sum[:]).then_inc(stored, 16)

            with pool.Fori(0, PAIRS) as i:
                for v in range(2):
                    store_y(2 * i + v, v)
            with pool.Fori(0, PAIRS) as i:
                for v in range(2):
                    store_out(2 * i + v, v, i)
                    store_y(NB + 2 * i + v, v)
            with pool.Fori(0, PAIRS) as i:
                for v in range(2):
                    store_out(NB + 2 * i + v, v, PAIRS + i)
            pool.wait_ge(stored, 16 * 2 * NB)

        @block.tensor
        def _(pe):
            def turn_pair(w, unit, v, turn):
                pe.wait_ge(norm_ready[v], turn + 1)
                pe.wait_ge(ht_ready[w], unit)
                for b in range(2):
                    last = nc.tensor.transpose(ps_turn[w][:, b * P:(b + 1) * P],
                                               x_norm[:, v, w * PW + b * C:w * PW + (b + 1) * C], ident[:])
                last.then_inc(turned[w], 1)

            def project(w, unit):
                pe.wait_ge(ht_ready[w], unit + 1)
                pe.wait_ge(proj_ready[w], unit)
                for b in range(2):
                    cols = slice(b * P, (b + 1) * P)
                    for n, (h, v) in enumerate(((ht_hi, v_lo), (ht_hi, v_hi), (ht_lo, v_hi))):
                        last = nc.tensor.matmul(ps_proj[w][:, b, :], h[:, w, cols], v[:],
                                                start=n == 0, stop=n == 2)
                last.then_inc(projected[w], 1)

            def hop(s, u, n):
                r = s % 2
                pe.wait_ge(summed[u], n)
                for jb in range(NB):
                    if jb in (0, NB // 2):
                        pe.wait_ge(a_ready[u], 2 * n + 1 + jb // (NB // 2))
                    if jb in (0, NB - 2, NB - 1):
                        rows = NB - 2 if jb == 0 else jb + 1
                        if s % HOPS:
                            pe.wait_ge(u_ready, inner_before(s) - NB + rows)
                        else:
                            for w in range(2):
                                pe.wait_ge(proj_ready[w], NB * (s // HOPS) + rows)
                    cols = slice(jb * P, (jb + 1) * P)
                    nc.tensor.matmul(ps_hop[u][:], a_hi[:, u, cols], u_lo[:, r, jb, :],
                                     start=jb == 0, stop=False)
                    nc.tensor.matmul(ps_hop[u][:], a_hi[:, u, cols], u_hi[:, r, jb, :],
                                     start=False, stop=False)
                    last = nc.tensor.matmul(ps_hop[u][:], a_lo[:, u, cols], u_hi[:, r, jb, :],
                                            start=False, stop=jb == NB - 1)
                last.then_inc(hop_done[u], 1)

            pe.wait_ge(ident_ready, 1)
            turn_pair(0, 0, 0, 0)
            pe.wait_ge(v_ready, 1)
            with pe.Fori(0, PAIRS) as i:
                for v in range(2):
                    unit = 2 * i + v
                    turn_pair(1, unit, v, i)
                    project(0, unit)
                    turn_pair(0, unit + 1, 1 - v, i + v)
                    project(1, unit)
            for s in range(STAGES):
                if s != HOPS - 1:
                    with pe.Fori(0, PAIRS) as i:
                        for u in range(2):
                            hop(s, u, PAIRS * s + i)
                    continue

                turn_pair(1, NB, 0, PAIRS)

                def turn(i, last):
                    for u in range(2):
                        unit = NB + 2 * i + u
                        hop(s, u, PAIRS * s + i)
                        for w in range(2):
                            project(w, unit)
                        if not (last and u == 1):
                            for w in range(2):
                                turn_pair(w, unit + 1, 1 - u, PAIRS + i + u)

                with pe.Fori(0, PAIRS - 1) as i:
                    turn(i, False)
                turn(PAIRS - 1, True)

        @block.scalar
        def _(act):
            def relu_turned(w, unit):
                act.wait_ge(turned[w], unit + 1)
                act.wait_ge(projected[w], unit)
                nc.scalar.activation(ht_hi[:, w, :], ps_turn[w][:, 0:PW], ACT.Relu
                                     ).then_inc(ht_hi_ready[w], 1)

            def std_dev(unit):
                act.wait_ge(stats_ready, unit + 1)
                nc.scalar.activation(std[:], mean_var[:, :, 1], ACT.Sqrt, bias=eps[:]
                                     ).then_inc(std_ready, 1)

            def proj_hi(write, ib, w, unit, v, turn):
                act.wait_ge(projected[w], unit + 1)
                nc.scalar.activation(pair_rows(u_hi, write, ib, w), ps_proj[w][:, :, 3 * C:4 * C], ACT.Copy)
                act.wait_ge(spilled[v], 16 * turn)
                nc.scalar.activation(pair_terms(v, w), ps_proj[w][:, :, 0:3 * C].rearrange(
                    "p b (k c) -> p k b c", k=3), ACT.Copy).then_inc(proj_hi_ready[w], 1)

            def split_hi(u, n):
                act.wait_ge(hop_done[u], n)
                for c in range(2):
                    blocks = 2 * n + u + 1
                    act.wait_ge(a_landed[c], 16 * blocks)
                    nc.scalar.activation(a_hi[:, u, c * CH:(c + 1) * CH], a_raw[:, c, :], ACT.Copy
                                         ).then_inc(a_hi_ready[u], 1)

            def hop_hi(s, u, n, ib):
                act.wait_ge(summed[u], n + 1)
                nc.scalar.activation(rows(u_hi, (s + 1) % 2, ib), u_sum[:], ACT.Copy
                                     ).then_inc(u_hi_ready, 1)

            act.wait_ge(eps_ready, 1)
            std_dev(0)
            act.wait_ge(w_summed, 1)
            nc.scalar.activation(v_hi[:], w_raw[:, 0:TERMS * C], ACT.Copy).then_inc(v_hi_ready, 1)
            relu_turned(0, 0)
            std_dev(1)

            def project_turn(i):
                for v in range(2):
                    unit = 2 * i + v
                    relu_turned(1, unit)
                    proj_hi(0, unit, 0, unit, v, i)
                    relu_turned(0, unit + 1)
                    std_dev(unit + 2)
                    proj_hi(0, unit, 1, unit, v, i)

            with act.Fori(0, PAIRS // 2) as i:
                project_turn(i)
            split_hi(0, 0)
            with act.Fori(PAIRS // 2, PAIRS) as i:
                project_turn(i)

            for s in range(STAGES):
                proj = s == HOPS - 1
                if proj:
                    relu_turned(1, NB)

                def turn(i, last):
                    n = PAIRS * s + i
                    for u in range(2):
                        ib = 2 * i + u
                        unit = NB + ib
                        end = last and u == 1
                        if not (s == STAGES - 1 and end):
                            split_hi(1 - u, n + u)
                        if proj and not last:
                            std_dev(unit + 2)
                        if not final(s):
                            hop_hi(s, u, n, ib)
                        if proj:
                            for w in range(2):
                                proj_hi((s + 1) % 2, ib, w, unit, u, PAIRS + i)
                            if not end:
                                for w in range(2):
                                    relu_turned(w, unit + 1)

                if final(s):
                    with act.Fori(0, PAIRS - 1) as i:
                        turn(i, False)
                    turn(PAIRS - 1, True)
                else:
                    with act.Fori(0, PAIRS) as i:
                        turn(i, False)

        @block.vector
        def _(dve):
            def batch_stats(unit, v, turn):
                dve.wait_ge(x_landed[v], 16 * (turn + 1))
                dve.wait_ge(stats_ready, unit)
                for b in range(HB):
                    last = nc.vector.bn_stats(bn[:, b, :], x_in[:, v, b * C:(b + 1) * C])
                last.then_inc(bn_ready, 1)

            def mean_and_var():
                for b in range(HB):
                    last = nc.vector.bn_aggr(mean_var[:, b, :], bn[:, b, :])
                last.then_inc(stats_ready, 1)

            def normalise(unit, v, turn):
                dve.wait_ge(std_ready, unit + 1)
                dve.wait_ge(norm_ready[1 - v], turn + v)
                nc.vector.reciprocal(rstd[:], std[:]).then_inc(rstd_ready, 1)
                if not (isinstance(turn, int) and turn == 0):
                    dve.wait_ge(turned[1], unit - 1)
                dve.wait_ge(rstd_ready, unit + 1)
                for b in range(HB):
                    cols = slice(b * C, (b + 1) * C)
                    last = nc.vector.tensor_scalar(x_norm[:, v, cols], x_in[:, v, cols],
                                                   mean_var[:, b, 0:1], rstd[:, b:b + 1],
                                                   ALU.subtract, ALU.mult)
                last.then_inc(norm_ready[v], 1)

            def turned_lo(w, unit):
                dve.wait_ge(ht_hi_ready[w], unit + 1)
                nc.vector.scalar_tensor_tensor(out=ht_lo[:, w, :], in0=ps_turn[w][:, 0:PW], scalar=0.0,
                                               in1=ht_hi[:, w, :].bitcast(F32), op0=ALU.max,
                                               op1=ALU.subtract).then_inc(ht_ready[w], 1)

            def proj_lo(write, ib, w, unit):
                dve.wait_ge(proj_hi_ready[w], unit + 1)
                nc.vector.tensor_tensor(pair_rows(u_lo, write, ib, w), ps_proj[w][:, :, 3 * C:4 * C],
                                        pair_rows(u_hi, write, ib, w).bitcast(F32), ALU.subtract
                                        ).then_inc(proj_ready[w], 1)

            def split_lo(u, n):
                for c in range(2):
                    cols = slice(c * CH, (c + 1) * CH)
                    dve.wait_ge(a_hi_ready[u], 2 * n + c + 1)
                    nc.vector.tensor_tensor(a_lo[:, u, cols], a_raw[:, c, :],
                                            a_hi[:, u, cols].bitcast(F32), ALU.subtract
                                            ).then_inc(a_ready[u], 1)

            def hop_sum(s, u, n, ib):
                dve.wait_ge(hop_done[u], n + 1)
                dve.wait_ge(y_landed[u], 16 * (n + 1))
                if final(s):
                    dve.wait_ge(stored, 16 * (NB * (s // HOPS) + ib))
                else:
                    dve.wait_ge(u_ready, inner_before(s) + ib)
                nc.vector.tensor_tensor(u_sum[:], ps_hop[u][:], y_in[:, u, :], ALU.add
                                        ).then_inc(summed[u], 1)
                if final(s):
                    m = n - PAIRS * s + PAIRS * (s // HOPS)
                    dve.wait_ge(res_landed[u], 16 * (m + 1))
                    dve.wait_ge(summed[u], n + 1)
                    nc.vector.tensor_tensor(u_sum[:], u_sum[:], x_res[:, u, :], ALU.add
                                            ).then_inc(out_ready[u], 1)
                else:
                    dve.wait_ge(u_hi_ready, inner_before(s) + ib + 1)
                    nc.vector.tensor_tensor(rows(u_lo, (s + 1) % 2, ib), u_sum[:],
                                            rows(u_hi, (s + 1) % 2, ib).bitcast(F32), ALU.subtract
                                            ).then_inc(u_ready, 1)

            batch_stats(0, 0, 0)
            dve.wait_ge(bn_ready, 1)
            mean_and_var()
            dve.wait_ge(w_landed, 16)
            nc.vector.tensor_tensor(w_raw[:, C:4 * C], w_raw[:, C:4 * C], w_raw[:, 4 * C:7 * C], ALU.add
                                    ).then_inc(w_summed, 1)
            normalise(0, 0, 0)
            batch_stats(1, 1, 0)
            dve.wait_ge(bn_ready, 2)
            dve.wait_ge(norm_ready[0], 1)
            mean_and_var()
            dve.wait_ge(v_hi_ready, 1)
            nc.vector.tensor_tensor(v_lo[:], w_raw[:, 0:4 * C], v_hi[:].bitcast(F32), ALU.subtract
                                    ).then_inc(v_ready, 1)
            turned_lo(0, 0)
            normalise(1, 1, 0)

            def project_turn(i):
                for v in range(2):
                    unit = 2 * i + v
                    batch_stats(unit + 2, v, i + 1)
                    dve.wait_ge(bn_ready, unit + 3)
                    dve.wait_ge(norm_ready[1 - v], i + 1 + v)
                    turned_lo(1, unit)
                    proj_lo(0, unit, 0, unit)
                    mean_and_var()
                    turned_lo(0, unit + 1)
                    normalise(unit + 2, v, i + 1)
                    proj_lo(0, unit, 1, unit)

            with dve.Fori(0, PAIRS // 2) as i:
                project_turn(i)
            split_lo(0, 0)
            with dve.Fori(PAIRS // 2, PAIRS) as i:
                project_turn(i)

            for s in range(STAGES):
                proj = s == HOPS - 1
                if final(s):
                    dve.wait_ge(u_ready, inner_before(s))
                if s == HOPS:
                    dve.wait_ge(stored, 16 * NB)

                if proj:
                    turned_lo(1, NB)

                def turn(i, last):
                    n = PAIRS * s + i
                    for u in range(2):
                        ib = 2 * i + u
                        unit = NB + ib
                        end = last and u == 1
                        if proj and not last:
                            batch_stats(unit + 2, u, PAIRS + i + 1)
                            dve.wait_ge(bn_ready, unit + 3)
                            dve.wait_ge(norm_ready[1 - u], PAIRS + i + 1 + u)
                        if not (s == STAGES - 1 and end):
                            split_lo(1 - u, n + u)
                        if proj and not last:
                            mean_and_var()
                            normalise(unit + 2, u, PAIRS + i + 1)
                        hop_sum(s, u, n, ib)
                        if proj:
                            for w in range(2):
                                proj_lo((s + 1) % 2, ib, w, unit)
                            if not end:
                                for w in range(2):
                                    turned_lo(w, unit + 1)

                if final(s):
                    with dve.Fori(0, PAIRS - 1) as i:
                        turn(i, False)
                    turn(PAIRS - 1, True)
                else:
                    with dve.Fori(0, PAIRS) as i:
                        turn(i, False)


def kernel(x, adj, L0_gnn_weight_1):
    import numpy as np
    import concourse.bacc as bacc
    from concourse.bass_utils import run_bass_kernel_spmd

    x_units = np.ascontiguousarray(
        x.reshape(2, HB, NB, P, C).transpose(0, 2, 3, 1, 4)).reshape(2 * NB, P, W)
    panels = np.ascontiguousarray(
        adj.reshape(NB, P, NB, P).transpose(0, 3, 2, 1)).reshape(NB, P, NB * P)
    weight = np.ascontiguousarray(L0_gnn_weight_1.transpose(0, 2, 1)).reshape(C, 7 * C)

    nc = bacc.Bacc("TRN2", target_bir_lowering=False, num_devices=1)
    arrays = {"x_units": x_units, "panels": panels, "weight": weight}
    args = [nc.dram_tensor(name, a.shape, F32, kind="ExternalInput").ap() for name, a in arrays.items()]
    out = nc.dram_tensor("out", (2 * NB, P, W), F32, kind="ExternalOutput").ap()
    build(nc, *args, out)
    got = run_bass_kernel_spmd(nc, [arrays], core_ids=[0]).results[0]["out"]
    return got.reshape(2, NB, P, HB, C).transpose(0, 3, 1, 2, 4).reshape(B, N, C)
```

```python
from contextlib import ExitStack

import concourse.bass as bass
import concourse.mybir as mybir

P = 128
B, N, C = 8, 2048, 128
NB = N // P
HB = B // 2
W = HB * C
PW = W // 2
TERMS = 4
HOPS = 3
STAGES = 2 * HOPS
PAIRS = NB // 2
CH = NB * P // 2
FIRST = NB * P // PAIRS
EPS = 1e-5

F32 = mybir.dt.float32
F32R = mybir.dt.float32r
ALU = mybir.AluOpType
ACT = mybir.ActivationFunctionType


def build(nc, x, adj, weight, out):
    ctx = ExitStack()
    with ctx:
        def sb(name, shape, dt=F32):
            return ctx.enter_context(nc.sbuf_tensor(name, shape, dt))

        def pb(name, shape):
            return ctx.enter_context(nc.psum_tensor(name, shape, F32))

        def sem(name):
            return ctx.enter_context(nc.semaphore(name))

        def sems(name):
            return [sem(f"{name}{slot}") for slot in range(2)]

        spill = nc.dram_tensor("y_spill", [2 * NB, P, 3 * W], F32, kind="Internal").ap()

        u_hi = sb("u_hi", [P, 2, NB, W], F32R)
        u_lo = sb("u_lo", [P, 2, NB, W], F32R)
        a_raw = sb("a_raw", [P, 2 * CH])
        a_hi = sb("a_hi", [P, 2, NB * P], F32R)
        a_lo = sb("a_lo", [P, 2, NB * P], F32R)
        y_in = sb("y_in", [P, 2, W])
        x_res = sb("x_res", [P, 2, W])
        u_sum = sb("u_sum", [P, W])
        x_in = sb("x_in", [P, 2, W])
        x_norm = sb("x_norm", [P, 2, W])
        ht_hi = sb("ht_hi", [P, 2, PW], F32R)
        ht_lo = sb("ht_lo", [P, 2, PW], F32R)
        y_out = sb("y_out", [P, 2, 3 * W])
        v_hi = sb("v_hi", [P, TERMS * C], F32R)
        v_lo = sb("v_lo", [P, TERMS * C], F32R)
        ident = sb("ident", [P, P])
        bn = sb("bn", [P, HB, 6])
        mean_var = sb("mean_var", [P, HB, 2])
        std = sb("std", [P, HB])
        rstd = sb("rstd", [P, HB])
        eps = sb("eps", [P, 1])
        eps_std = sb("eps_std", [P, 1])
        w_raw = y_out[:, 0, :]

        ps_hop = [pb(f"ps_hop{s}", [P, W]) for s in range(2)]
        ps_turn = [pb(f"ps_turn{s}", [P, 512]) for s in range(2)]
        ps_proj = [pb(f"ps_proj{s}", [P, 2, TERMS * C]) for s in range(2)]

        w_landed = sem("w_landed")
        w_summed = sem("w_summed")
        v_hi_ready = sem("v_hi_ready")
        v_ready = sem("v_ready")
        ident_zero = sem("ident_zero")
        ident_ready = sem("ident_ready")
        eps_ready = sem("eps_ready")
        x_landed = sems("x_landed")
        bn_ready = sem("bn_ready")
        stats_ready = sem("stats_ready")
        std_ready = sem("std_ready")
        rstd_ready = sem("rstd_ready")
        norm_ready = sems("norm_ready")
        centred = sem("centred")
        norm2_ready = sems("norm2_ready")
        turned = sems("turned")
        ht_hi_ready = sems("ht_hi_ready")
        ht_ready = sems("ht_ready")
        projected = [sem(f"projected{b}") for b in range(HB)]
        proj_hi_ready = [sem(f"proj_hi_ready{b}") for b in range(HB)]
        proj_ready = [sem(f"proj_ready{b}") for b in range(HB)]
        spilled = sems("spilled")
        a_landed = sems("a_landed")
        a_hi_ready = sems("a_hi_ready")
        a_ready = sems("a_ready")
        first_hi = sem("first_hi")
        first_lo = sem("first_lo")
        hop_done = sems("hop_done")
        y_landed = sems("y_landed")
        res_landed = sems("res_landed")
        summed = sems("summed")
        u_hi_ready = sem("u_hi_ready")
        u_ready = sem("u_ready")
        y_added = sems("y_added")
        out_ready = sems("out_ready")
        stored = sem("stored")

        def final(s):
            return s % HOPS == HOPS - 1

        def inner_before(s):
            return NB * (s - s // HOPS)

        def sums(s, i):
            if final(s):
                return PAIRS * (s - s // HOPS), PAIRS * (s // HOPS) + i
            return PAIRS * (s - s // HOPS) + i, PAIRS * (s // HOPS)

        def zero(count):
            return isinstance(count, int) and count == 0

        def peeled(s):
            return 1 if s in (0, HOPS - 1) else 0

        def ds(start, size):
            return bass.ds(start, size)

        def rows(tensor, copy, ib):
            return tensor[:, copy, ds(ib, 1), :].rearrange("p a w -> p (a w)")

        def batch_rows(tensor, copy, ib, b):
            return tensor[:, copy, ds(ib, 1), b * C:(b + 1) * C].rearrange("p a c -> p (a c)")

        def batch_terms(v, b):
            return y_out[:, v, :].rearrange("p (k b c) -> p k b c", k=3, b=HB)[:, :, b]

        block = ctx.enter_context(nc.Block())

        @block.sync
        def _(sp):
            def load_x(unit, v, turn):
                if turn is not None:
                    sp.wait_ge(norm_ready[v], turn)
                    sp.wait_ge(norm2_ready[v], turn)
                sp.dma_start(x_in[:, v, :], x[ds(unit, 1), :, :].rearrange("a p w -> (a p) w")
                             ).then_inc(x_landed[v], 16)

            def load_a(ib, u, turn):
                for c in range(2):
                    if turn is not None:
                        sp.wait_ge(a_ready[u], 2 * turn + c + 1)
                    sp.dma_start(a_raw[:, c * CH:(c + 1) * CH],
                                 adj[ds(ib, 1), :, c * CH:(c + 1) * CH].rearrange("a p w -> (a p) w")
                                 ).then_inc(a_landed[c], 16)

            def load_y(s, ib, u):
                k = HOPS - 1 - s % HOPS
                unit = NB * (s // HOPS) + ib
                sp.dma_start(y_in[:, u, :],
                             spill[ds(unit, 1), :, k * W:(k + 1) * W].rearrange("a p w -> (a p) w")
                             ).then_inc(y_landed[u], 16)
                if final(s):
                    sp.dma_start(x_res[:, u, :], x[ds(unit, 1), :, :].rearrange("a p w -> (a p) w")
                                 ).then_inc(res_landed[u], 16)

            load_x(0, 0, None)
            sp.dma_start(w_raw[:, 0:7 * C], weight).then_inc(w_landed, 16)
            load_x(1, 1, None)
            load_a(0, 0, None)
            with sp.Fori(0, PAIRS) as i:
                for v in range(2):
                    load_x(2 * i + 2 + v, v, i + 1)
            load_x(NB + 2, 0, PAIRS + 1)
            sp.wait_ge(first_lo, PAIRS)
            load_a(1, 0, 0)

            for s in range(STAGES):
                n0 = PAIRS * s
                proj = s == HOPS - 1
                if s % HOPS == 0:
                    for v in range(2):
                        sp.wait_ge(spilled[v], 16 * PAIRS * (s // HOPS + 1))
                if s == 0:
                    load_y(s, 0, 0)
                if not zero(sums(s, 0)[0]):
                    sp.wait_ge(summed[1], sums(s, 0)[0])
                if not zero(sums(s, 0)[1]):
                    sp.wait_ge(out_ready[1], sums(s, 0)[1])

                def turn(i, rest):
                    n = n0 + i
                    for u in range(2):
                        if proj and (rest > 1 or (rest == 1 and u == 0)):
                            load_x(NB + 2 * i + 3 + u, 1 - u, PAIRS + i + 1 + u)
                        if rest:
                            load_a(2 * i + 2 + u, 1 - u, n + u)
                        elif s < STAGES - 1:
                            load_a(u, 1 - u, n + u)
                        if u == 0 or rest:
                            nxt = (s, 2 * i + 1 + u)
                        elif s < STAGES - 1:
                            nxt = (s + 1, 0)
                        else:
                            break
                        if nxt[0] % HOPS == 0 and nxt[0] != s:
                            for v in range(2):
                                sp.wait_ge(spilled[v], 16 * PAIRS * (nxt[0] // HOPS + 1))
                        if final(s):
                            if not zero(sums(s, i)[1] + u):
                                sp.wait_ge(out_ready[1 - u], sums(s, i)[1] + u)
                        elif not zero(sums(s, i)[0] + u):
                            sp.wait_ge(summed[1 - u], sums(s, i)[0] + u)
                        load_y(*nxt, 1 - u)

                ahead = 2 if proj else 1
                if peeled(s):
                    turn(0, ahead)
                with sp.Fori(peeled(s), PAIRS - ahead) as i:
                    turn(i, ahead)
                for rest in reversed(range(ahead)):
                    turn(PAIRS - 1 - rest, rest)

        @block.gpsimd
        def _(pool):
            nc.gpsimd.memset(ident[:], 0.0).then_inc(ident_zero, 1)
            nc.gpsimd.memset(eps[:], EPS).then_inc(eps_ready, 1)
            pool.wait_ge(ident_zero, 1)
            nc.gpsimd.affine_select(out=ident[:], in_=ident[:], compare_op=ALU.not_equal, fill=1.0,
                                    base=0, pattern=[[-1, P]], channel_multiplier=1
                                    ).then_inc(ident_ready, 1)

            def store_y(unit, v):
                for b in range(HB):
                    pool.wait_ge(proj_hi_ready[b], unit + 1)
                pool.dma_start(spill[ds(unit, 1), :, :].rearrange("a p w -> (a p) w"),
                               y_out[:, v, :]).then_inc(spilled[v], 16)

            def normalise(unit, v, turn):
                cols = slice(PW, 2 * PW)
                by_batch = "p (b c) -> p b c"
                x_batches = x_in[:, v, cols].rearrange(by_batch, b=2)
                norm_batches = x_norm[:, v, cols].rearrange(by_batch, b=2)
                if not zero(turn):
                    pool.wait_ge(turned[1], unit - 1)
                pool.wait_ge(rstd_ready, unit + 1)
                nc.gpsimd.tensor_tensor(norm_batches, x_batches,
                                        mean_var[:, 2:4, 0:1].to_broadcast([P, 2, C]),
                                        ALU.subtract).then_inc(centred, 1)
                pool.wait_ge(centred, unit + 1)
                nc.gpsimd.tensor_tensor(norm_batches, norm_batches,
                                        rstd[:, 2:4].rearrange("p (b a) -> p b a", a=1).to_broadcast([P, 2, C]),
                                        ALU.mult).then_inc(norm2_ready[v], 1)

            def first_split_lo(i):
                pool.wait_ge(first_hi, i + 1)
                cols = ds(i * FIRST, FIRST)
                nc.gpsimd.tensor_tensor(a_lo[:, 0, cols], a_raw[:, cols],
                                        a_hi[:, 0, cols].bitcast(F32), ALU.subtract
                                        ).then_inc(first_lo, 1)

            pool.sem_inc(a_ready[0], 2)

            def project_turn(i):
                for v in range(2):
                    normalise(2 * i + v + 2, v, i + 1)
                    if v == 0:
                        first_split_lo(i)
                    store_y(2 * i + v, v)

            normalise(0, 0, 0)
            normalise(1, 1, 0)
            with pool.Fori(0, PAIRS) as i:
                project_turn(i)

            def last_hop_turn(i, last):
                for v in range(2):
                    if not last:
                        normalise(NB + 2 * i + v + 2, v, PAIRS + i + 1)
                    store_y(NB + 2 * i + v, v)

            with pool.Fori(0, PAIRS - 1) as i:
                last_hop_turn(i, False)
            last_hop_turn(PAIRS - 1, True)

        @block.tensor
        def _(pe):
            def turn_pair(w, unit, v, turn):
                pe.wait_ge((norm_ready, norm2_ready)[w][v], turn + 1)
                if not zero(unit):
                    pe.wait_ge(ht_ready[w], unit)
                for b in range(2):
                    last = nc.tensor.transpose(ps_turn[w][:, b * P:(b + 1) * P],
                                               x_norm[:, v, w * PW + b * C:w * PW + (b + 1) * C], ident[:])
                last.then_inc(turned[w], 1)

            def project(w, unit):
                pe.wait_ge(ht_ready[w], unit + 1)
                for b in range(2):
                    cols = slice(b * P, (b + 1) * P)
                    if not zero(unit):
                        pe.wait_ge(proj_ready[2 * w + b], unit)
                    for n, (h, v) in enumerate(((ht_hi, v_lo), (ht_hi, v_hi), (ht_lo, v_hi))):
                        last = nc.tensor.matmul(ps_proj[w][:, b, :], h[:, w, cols], v[:],
                                                start=n == 0, stop=n == 2)
                    last.then_inc(projected[2 * w + b], 1)

            def hop(s, u, i):
                r = s % 2
                n = PAIRS * s + i
                if not zero(sums(s, i)[0]):
                    pe.wait_ge(summed[u], sums(s, i)[0])
                if not zero(sums(s, i)[1]):
                    pe.wait_ge(out_ready[u], sums(s, i)[1])
                for jb in range(NB):
                    if jb in (0, NB // 2):
                        pe.wait_ge(a_ready[u], 2 * n + 1 + jb // (NB // 2))
                    if jb in (0, NB - 2, NB - 1):
                        ready_rows = NB - 2 if jb == 0 else jb + 1
                        if s % HOPS:
                            pe.wait_ge(u_ready, inner_before(s) - NB + ready_rows)
                        else:
                            pe.wait_ge(proj_ready[HB - 1], NB * (s // HOPS) + ready_rows)
                    cols = slice(jb * P, (jb + 1) * P)
                    nc.tensor.matmul(ps_hop[u][:], a_hi[:, u, cols], u_lo[:, r, jb, :],
                                     start=jb == 0, stop=False)
                    nc.tensor.matmul(ps_hop[u][:], a_hi[:, u, cols], u_hi[:, r, jb, :],
                                     start=False, stop=False)
                    last = nc.tensor.matmul(ps_hop[u][:], a_lo[:, u, cols], u_hi[:, r, jb, :],
                                            start=False, stop=jb == NB - 1)
                last.then_inc(hop_done[u], 1)

            pe.wait_ge(ident_ready, 1)
            turn_pair(0, 0, 0, 0)
            turn_pair(1, 0, 0, 0)
            pe.wait_ge(v_ready, 1)

            def project_turn(i):
                for v in range(2):
                    for w in range(2):
                        turn_pair(w, 2 * i + v + 1, 1 - v, i + v)
                        project(w, 2 * i + v)

            project_turn(0)
            with pe.Fori(1, PAIRS) as i:
                project_turn(i)
            pe.wait_ge(first_lo, PAIRS)
            for s in range(STAGES):
                if s != HOPS - 1:
                    if peeled(s):
                        for u in range(2):
                            hop(s, u, 0)
                    with pe.Fori(peeled(s), PAIRS) as i:
                        for u in range(2):
                            hop(s, u, i)
                    continue

                def turn(i, last):
                    for u in range(2):
                        unit = NB + 2 * i + u
                        hop(s, u, i)
                        for w in range(2):
                            project(w, unit)
                        if not (last and u == 1):
                            for w in range(2):
                                turn_pair(w, unit + 1, 1 - u, PAIRS + i + u)

                turn(0, False)
                with pe.Fori(1, PAIRS - 1) as i:
                    turn(i, False)
                turn(PAIRS - 1, True)

        @block.scalar
        def _(act):
            def relu_turned(w, unit):
                act.wait_ge(turned[w], unit + 1)
                if not zero(unit):
                    act.wait_ge(projected[2 * w + 1], unit)
                nc.scalar.activation(ht_hi[:, w, :], ps_turn[w][:, 0:PW], ACT.Relu
                                     ).then_inc(ht_hi_ready[w], 1)

            def std_dev(unit):
                act.wait_ge(stats_ready, unit + 1)
                nc.scalar.activation(std[:], mean_var[:, :, 1], ACT.Sqrt, bias=eps[:]
                                     ).then_inc(std_ready, 1)

            def proj_hi(write, ib, w, unit, v, turn):
                if not zero(turn):
                    act.wait_ge(spilled[v], 16 * turn)
                for b in range(2):
                    bank = ps_proj[w][:, b, :]
                    act.wait_ge(projected[2 * w + b], unit + 1)
                    nc.scalar.activation(batch_rows(u_hi, write, ib, 2 * w + b), bank[:, 3 * C:4 * C], ACT.Copy)
                    nc.scalar.activation(batch_terms(v, 2 * w + b),
                                         bank[:, 0:3 * C].rearrange("p (k c) -> p k c", k=3), ACT.Copy
                                         ).then_inc(proj_hi_ready[2 * w + b], 1)

            def split_hi(u, n):
                if not zero(n):
                    act.wait_ge(hop_done[u], n)
                for c in range(2):
                    blocks = 2 * n + u + 1
                    act.wait_ge(a_landed[c], 16 * blocks)
                    nc.scalar.activation(a_hi[:, u, c * CH:(c + 1) * CH], a_raw[:, c * CH:(c + 1) * CH], ACT.Copy
                                         ).then_inc(a_hi_ready[u], 1)

            def hop_hi(s, u, i, ib):
                act.wait_ge(summed[u], sums(s, i)[0] + 1)
                nc.scalar.activation(rows(u_hi, (s + 1) % 2, ib), u_sum[:], ACT.Copy
                                     ).then_inc(u_hi_ready, 1)

            def store_out(unit, u, m):
                act.wait_ge(out_ready[u], m + 1)
                act.dma_start(out[ds(unit, 1), :, :].rearrange("a p w -> (a p) w"),
                              u_sum[:]).then_inc(stored, 16)

            act.wait_ge(eps_ready, 1)
            nc.scalar.activation(eps_std[:], eps[:], ACT.Sqrt)
            std_dev(0)
            act.wait_ge(w_summed, 1)
            nc.scalar.activation(v_hi[:], w_raw[:, 0:TERMS * C], ACT.Copy).then_inc(v_hi_ready, 1)
            relu_turned(0, 0)
            relu_turned(1, 0)
            std_dev(1)

            def project_turn(i):
                cols = ds(i * FIRST, FIRST)
                nc.scalar.activation(a_hi[:, 0, cols], a_raw[:, cols], ACT.Copy).then_inc(first_hi, 1)
                for v in range(2):
                    unit = 2 * i + v
                    for w in range(2):
                        relu_turned(w, unit + 1)
                        if w == 0:
                            std_dev(unit + 2)
                        proj_hi(0, unit, w, unit, v, i)

            for c in range(2):
                act.wait_ge(a_landed[c], 16)
            project_turn(0)
            with act.Fori(1, PAIRS) as i:
                project_turn(i)
            act.sem_inc(a_hi_ready[0], 2)

            for s in range(STAGES):
                proj = s == HOPS - 1

                def turn(i, last):
                    n = PAIRS * s + i
                    for u in range(2):
                        ib = 2 * i + u
                        unit = NB + ib
                        end = last and u == 1
                        if proj and not last:
                            std_dev(unit + 2)
                        if not (s == STAGES - 1 and end):
                            split_hi(1 - u, n + u)
                        if final(s):
                            store_out(NB * (s // HOPS) + ib, u, PAIRS * (s // HOPS) + i)
                        else:
                            hop_hi(s, u, i, ib)
                        if proj:
                            for w in range(2):
                                proj_hi((s + 1) % 2, ib, w, unit, u, PAIRS + i)
                            if not end:
                                for w in range(2):
                                    relu_turned(w, unit + 1)

                if final(s):
                    with act.Fori(0, PAIRS - 1) as i:
                        turn(i, False)
                    turn(PAIRS - 1, True)
                else:
                    if peeled(s):
                        turn(0, False)
                    with act.Fori(peeled(s), PAIRS) as i:
                        turn(i, False)
            act.wait_ge(stored, 16 * 2 * NB)

        @block.vector
        def _(dve):
            def batch_stats(unit, v, turn, batches=range(HB)):
                for b in batches:
                    if b == 0:
                        dve.wait_ge(x_landed[v], 16 * (turn + 1))
                        if not zero(unit):
                            dve.wait_ge(stats_ready, unit)
                    nc.vector.bn_stats(bn[:, b, :], x_in[:, v, b * C:(b + 1) * C]).then_inc(bn_ready, 1)

            def mean_and_var():
                for b in range(HB):
                    last = nc.vector.bn_aggr(mean_var[:, b, :], bn[:, b, :])
                last.then_inc(stats_ready, 1)

            def for_mean_and_var(unit, v, turn):
                dve.wait_ge(bn_ready, HB * (unit + 1))
                dve.wait_ge(norm_ready[1 - v], turn + v)
                dve.wait_ge(norm2_ready[1 - v], turn + v)

            def invert_std(unit):
                dve.wait_ge(std_ready, unit + 1)
                nc.vector.reciprocal(rstd[:], std[:]).then_inc(rstd_ready, 1)

            def normalise(unit, v, turn, b):
                if b == 0:
                    if not zero(turn):
                        dve.wait_ge(turned[0], unit - 1)
                    dve.wait_ge(rstd_ready, unit + 1)
                cols = slice(b * C, (b + 1) * C)
                step = nc.vector.tensor_scalar(x_norm[:, v, cols], x_in[:, v, cols],
                                               mean_var[:, b, 0:1], rstd[:, b:b + 1],
                                               ALU.subtract, ALU.mult)
                if b == 1:
                    step.then_inc(norm_ready[v], 1)

            def turned_lo(w, unit):
                dve.wait_ge(ht_hi_ready[w], unit + 1)
                nc.vector.scalar_tensor_tensor(out=ht_lo[:, w, :], in0=ps_turn[w][:, 0:PW], scalar=0.0,
                                               in1=ht_hi[:, w, :].bitcast(F32), op0=ALU.max,
                                               op1=ALU.subtract).then_inc(ht_ready[w], 1)

            def proj_lo(write, ib, b, unit):
                dve.wait_ge(proj_hi_ready[b], unit + 1)
                nc.vector.tensor_tensor(batch_rows(u_lo, write, ib, b),
                                        ps_proj[b // 2][:, b % 2, 3 * C:4 * C],
                                        batch_rows(u_hi, write, ib, b).bitcast(F32),
                                        ALU.subtract).then_inc(proj_ready[b], 1)

            def split_lo(u, n):
                for c in range(2):
                    cols = slice(c * CH, (c + 1) * CH)
                    dve.wait_ge(a_hi_ready[u], 2 * n + c + 1)
                    nc.vector.tensor_tensor(a_lo[:, u, cols], a_raw[:, c * CH:(c + 1) * CH],
                                            a_hi[:, u, cols].bitcast(F32), ALU.subtract
                                            ).then_inc(a_ready[u], 1)

            def hop_sum(s, u, i, ib):
                n = PAIRS * s + i
                dve.wait_ge(y_landed[u], 16 * (n + 1))
                if final(s):
                    m = sums(s, i)[1]
                    dve.wait_ge(res_landed[u], 16 * (m + 1))
                    nc.vector.tensor_tensor(y_in[:, u, :], y_in[:, u, :], x_res[:, u, :], ALU.add
                                            ).then_inc(y_added[u], 1)
                    dve.wait_ge(y_added[u], m + 1)
                    stores = NB * (s // HOPS) + ib
                    if not zero(stores):
                        dve.wait_ge(stored, 16 * stores)
                    dve.wait_ge(hop_done[u], n + 1)
                    nc.vector.tensor_tensor(u_sum[:], ps_hop[u][:], y_in[:, u, :], ALU.add
                                            ).then_inc(out_ready[u], 1)
                    return
                if not zero(inner_before(s) + ib):
                    dve.wait_ge(u_ready, inner_before(s) + ib)
                dve.wait_ge(hop_done[u], n + 1)
                nc.vector.tensor_tensor(u_sum[:], ps_hop[u][:], y_in[:, u, :], ALU.add
                                        ).then_inc(summed[u], 1)
                dve.wait_ge(u_hi_ready, inner_before(s) + ib + 1)
                nc.vector.tensor_tensor(rows(u_lo, (s + 1) % 2, ib), u_sum[:],
                                        rows(u_hi, (s + 1) % 2, ib).bitcast(F32), ALU.subtract
                                        ).then_inc(u_ready, 1)

            batch_stats(0, 0, 0)
            dve.wait_ge(bn_ready, HB)
            mean_and_var()
            dve.wait_ge(w_landed, 16)
            nc.vector.tensor_tensor(w_raw[:, C:4 * C], w_raw[:, C:4 * C], w_raw[:, 4 * C:7 * C], ALU.add
                                    ).then_inc(w_summed, 1)
            invert_std(0)
            for b in range(2):
                normalise(0, 0, 0, b)
            dve.wait_ge(v_hi_ready, 1)
            nc.vector.tensor_tensor(v_lo[:], w_raw[:, 0:4 * C], v_hi[:].bitcast(F32), ALU.subtract
                                    ).then_inc(v_ready, 1)
            batch_stats(1, 1, 0)
            for_mean_and_var(1, 1, 0)
            turned_lo(0, 0)
            mean_and_var()
            turned_lo(1, 0)
            invert_std(1)
            for b in range(2):
                normalise(1, 1, 0, b)
            batch_stats(2, 0, 1)
            dve.wait_ge(bn_ready, 3 * HB)
            dve.wait_ge(norm_ready[1], 1)
            dve.wait_ge(norm2_ready[1], 1)
            mean_and_var()

            def project_turn(i):
                for v in range(2):
                    unit = 2 * i + v
                    later = (unit + 3, 1 - v, i + 1 + v)
                    turned_lo(0, unit + 1)
                    invert_std(unit + 2)
                    normalise(unit + 2, v, i + 1, 0)
                    proj_lo(0, unit, 0, unit)
                    normalise(unit + 2, v, i + 1, 1)
                    proj_lo(0, unit, 1, unit)
                    batch_stats(*later, (0, 1, 2))
                    turned_lo(1, unit + 1)
                    batch_stats(*later, (3,))
                    for_mean_and_var(*later)
                    proj_lo(0, unit, 2, unit)
                    mean_and_var()
                    proj_lo(0, unit, 3, unit)

            with dve.Fori(0, PAIRS) as i:
                project_turn(i)

            for s in range(STAGES):
                proj = s == HOPS - 1
                if final(s):
                    dve.wait_ge(u_ready, inner_before(s))
                if s == HOPS:
                    dve.wait_ge(stored, 16 * NB)

                def turn(i, rest):
                    n = PAIRS * s + i
                    for u in range(2):
                        ib = 2 * i + u
                        unit = NB + ib
                        end = rest == 0 and u == 1
                        stats = proj and (rest > 1 or (rest == 1 and u == 0))
                        if proj and rest:
                            invert_std(unit + 2)
                            for b in range(2):
                                normalise(unit + 2, u, PAIRS + i + 1, b)
                        if stats:
                            batch_stats(unit + 3, 1 - u, PAIRS + i + 1 + u)
                            for_mean_and_var(unit + 3, 1 - u, PAIRS + i + 1 + u)
                        if not (s == STAGES - 1 and end):
                            split_lo(1 - u, n + u)
                        if stats:
                            mean_and_var()
                        hop_sum(s, u, i, ib)
                        if proj:
                            for b in range(HB):
                                proj_lo((s + 1) % 2, ib, b, unit)
                            if not end:
                                for w in range(2):
                                    turned_lo(w, unit + 1)

                ahead = 2 if proj else 1 if final(s) else 0
                if peeled(s):
                    turn(0, max(ahead, 1))
                with dve.Fori(peeled(s), PAIRS - ahead) as i:
                    turn(i, max(ahead, 1))
                for rest in reversed(range(ahead)):
                    turn(PAIRS - 1 - rest, rest)


def kernel(x, adj, L0_gnn_weight_1):
    import numpy as np
    import concourse.bacc as bacc
    from concourse.bass_utils import run_bass_kernel_spmd

    x_units = np.ascontiguousarray(
        x.reshape(2, HB, NB, P, C).transpose(0, 2, 3, 1, 4)).reshape(2 * NB, P, W)
    panels = np.ascontiguousarray(
        adj.reshape(NB, P, NB, P).transpose(0, 3, 2, 1)).reshape(NB, P, NB * P)
    weight = np.ascontiguousarray(L0_gnn_weight_1.transpose(0, 2, 1)).reshape(C, 7 * C)

    nc = bacc.Bacc("TRN2", target_bir_lowering=False, num_devices=1)
    arrays = {"x_units": x_units, "panels": panels, "weight": weight}
    args = [nc.dram_tensor(name, a.shape, F32, kind="ExternalInput").ap() for name, a in arrays.items()]
    out = nc.dram_tensor("out", (2 * NB, P, W), F32, kind="ExternalOutput").ap()
    build(nc, *args, out)
    got = run_bass_kernel_spmd(nc, [arrays], core_ids=[0]).results[0]["out"]
    return got.reshape(2, NB, P, HB, C).transpose(0, 3, 1, 2, 4).reshape(B, N, C)
```
